# Optimizing a Trainium2 kernel written in Bass

```python
import numpy as np
import jax
import jax.numpy as jnp

def _softmax(x, axis=-1):
    return jax.nn.softmax(x, axis=axis)

def _gelu(x):
    return jax.nn.gelu(x, approximate=True)

def _silu(x):
    return jax.nn.silu(x)

def _sigmoid(x):
    return jax.nn.sigmoid(x)

def _layernorm(x, axis=-1, eps=1e-05):
    m = jnp.mean(x, axis=axis, keepdims=True)
    v = jnp.var(x, axis=axis, keepdims=True)
    return (x - m) / jnp.sqrt(v + eps)

def _scatter_add(tgt, idx, src, axis=0):
    return tgt.at[idx].add(src)

def _segment_sum(src, seg, n):
    return jax.ops.segment_sum(src, seg, n)
kernel_name = 'mk_prb_d2_jaxref_r8_552ec3'

def setup_inputs(seed: int=0):
    np.random.seed(seed)
    _w = jnp.asarray

    def _L0_attn_setup():
        import jax, jax.numpy as jnp
        import numpy as np
        N_HEADS = 32
        N_KV_HEADS = 8
        HEAD_DIM = 64
        D_MODEL = 256
        SLIDING_WINDOW = 64
        ROPE_THETA = 10000.0
        PAST_LENGTH = 0
        EPS = 1e-06

        def _rms_norm(x, w):
            xf = x.astype(jnp.float32)
            rms = jax.lax.rsqrt(jnp.mean(xf * xf, axis=-1, keepdims=True) + EPS)
            return (xf * rms).astype(x.dtype) * w

        def _rope(q, k, past_length):
            s, d = (q.shape[2], q.shape[3])
            inv_freq = 1.0 / ROPE_THETA ** (jnp.arange(0, d, 2, dtype=jnp.float32) / d)
            pos = jnp.arange(s, dtype=jnp.float32) + past_length
            ang = pos[:, None] * inv_freq[None, :]
            emb = jnp.concatenate([ang, ang], axis=-1)
            cos, sin = (jnp.cos(emb), jnp.sin(emb))

            def rot_half(x):
                x1, x2 = jnp.split(x, 2, axis=-1)
                return jnp.concatenate([-x2, x1], axis=-1)
            q = q * cos + rot_half(q) * sin
            k = k * cos + rot_half(k) * sin
            return (q, k)

        def _sliding_mask(seq_len, total_len, past_length):
            q_idx = jnp.arange(seq_len)[:, None]
            k_idx = jnp.arange(total_len)[None, :]
            causal = q_idx + past_length >= k_idx
            window = q_idx + past_length - k_idx < SLIDING_WINDOW
            keep = causal & window
            return jnp.where(keep, 0.0, -jnp.inf).astype(jnp.float32)[None, None]
        key = jax.random.key(seed)
        k1, k2, k3 = jax.random.split(key, 3)
        B, S = (1, 256)
        q_size = N_HEADS * HEAD_DIM
        kv_size = N_KV_HEADS * HEAD_DIM
        return {'x': jax.random.normal(k1, (B, S, D_MODEL), dtype=jnp.float32), 'w_qkv': jax.random.normal(k2, (q_size + 2 * kv_size, D_MODEL), dtype=jnp.float32) * D_MODEL ** (-0.5), 'w_out': jax.random.normal(k3, (D_MODEL, q_size), dtype=jnp.float32) * q_size ** (-0.5), 'q_norm_w': jnp.ones((HEAD_DIM,), dtype=jnp.float32), 'k_norm_w': jnp.ones((HEAD_DIM,), dtype=jnp.float32)}
    _L0_attn_in = _L0_attn_setup()

    def _L0_ffn_setup():
        import jax, jax.numpy as jnp
        import numpy as np
        DIM = 256
        HID = 704
        ZERO_POINT = 128.0

        def _qlinear(x, wq, scale):
            W = (wq.astype(jnp.float32) - ZERO_POINT) * scale[:, None]
            return jnp.einsum('bsd,hd->bsh', x, W)
        key = jax.random.key(seed)
        ks = jax.random.split(key, 7)
        B, S = (4, 256)
        sg = jax.random.uniform(ks[1], (HID,)) * (0.02 / np.sqrt(DIM)) + 0.0001
        su = jax.random.uniform(ks[3], (HID,)) * (0.02 / np.sqrt(DIM)) + 0.0001
        sd = jax.random.uniform(ks[5], (DIM,)) * (0.02 / np.sqrt(HID)) + 0.0001
        return {'x': jax.random.normal(ks[0], (B, S, DIM), dtype=jnp.float32), 'wq_gate': jax.random.randint(ks[2], (HID, DIM), 0, 32, dtype=jnp.int32), 's_gate': sg, 'wq_up': jax.random.randint(ks[4], (HID, DIM), 0, 32, dtype=jnp.int32), 's_up': su, 'wq_down': jax.random.randint(ks[6], (DIM, HID), 0, 32, dtype=jnp.int32), 's_down': sd}
    _L0_ffn_in = _L0_ffn_setup()

    def _L1_attn_setup():
        import jax, jax.numpy as jnp
        import numpy as np
        NUM_HEADS = 16
        LN_EPS = 1e-05

        def _rope(x):
            S, D = (x.shape[-2], x.shape[-1])
            rot = D // 2
            inv_freq = 1.0 / 10000.0 ** (jnp.arange(0, rot, 2, dtype=jnp.float32) / rot)
            ang = jnp.arange(S, dtype=jnp.float32)[:, None] * inv_freq[None, :]
            ang = jnp.repeat(ang, 2, axis=-1)
            cos, sin = (jnp.cos(ang), jnp.sin(ang))
            xr, xp = (x[..., :rot], x[..., rot:])
            x1, x2 = (xr[..., 0::2], xr[..., 1::2])
            rot_half = jnp.stack((-x2, x1), axis=-1).reshape(xr.shape)
            xr = xr * cos + rot_half * sin
            return jnp.concatenate([xr, xp], axis=-1)
        key = jax.random.key(seed)
        k1, k2, k3 = jax.random.split(key, 3)
        B, S, D = (4, 256, 256)
        X = jax.random.normal(k1, (B, S, D), dtype=jnp.float32)
        ln_w = jnp.ones((D,), dtype=jnp.float32)
        ln_b = jnp.zeros((D,), dtype=jnp.float32)
        W_in = jax.random.normal(k2, (D, 3 * D), dtype=jnp.float32) * 0.02
        W_out = jax.random.normal(k3, (D, D), dtype=jnp.float32) * 0.02
        return {'X': X, 'ln_w': ln_w, 'ln_b': ln_b, 'W_in': W_in, 'W_out': W_out}
    _L1_attn_in = _L1_attn_setup()

    def _L1_ffn_setup():
        import jax, jax.numpy as jnp
        import numpy as np
        B, S, D = (4, 512, 256)
        DFF = 4 * D
        CAPACITY = 0.125
        K = int(CAPACITY * S)
        key = jax.random.key(seed)
        ks = jax.random.split(key, 8)
        sc = 1.0 / np.sqrt(D)
        return {'x': jax.random.normal(ks[0], (B, S, D), dtype=jnp.float32), 'W_r': jax.random.normal(ks[1], (D, 1), dtype=jnp.float32) * sc, 'b_r': jnp.zeros((1,), dtype=jnp.float32), 'W1': jax.random.normal(ks[2], (D, DFF), dtype=jnp.float32) * sc, 'b1': jnp.zeros((DFF,), dtype=jnp.float32), 'W2': jax.random.normal(ks[3], (DFF, D), dtype=jnp.float32) * (1.0 / np.sqrt(DFF)), 'b2': jnp.zeros((D,), dtype=jnp.float32), 'position_ids': jnp.arange(B * S, dtype=jnp.int64 if jax.config.jax_enable_x64 else jnp.int32).reshape(B, S), 'cache_position': jnp.arange(S, dtype=jnp.int64 if jax.config.jax_enable_x64 else jnp.int32)}
    _L1_ffn_in = _L1_ffn_setup()
    _d = {'L0_attn_x': _L0_attn_in['x'], 'L0_attn_w_qkv': _L0_attn_in['w_qkv'], 'L0_attn_w_out': _L0_attn_in['w_out'], 'L0_attn_q_norm_w': _L0_attn_in['q_norm_w'], 'L0_attn_k_norm_w': _L0_attn_in['k_norm_w'], 'L0_ffn_wq_gate': _L0_ffn_in['wq_gate'], 'L0_ffn_s_gate': _L0_ffn_in['s_gate'], 'L0_ffn_wq_up': _L0_ffn_in['wq_up'], 'L0_ffn_s_up': _L0_ffn_in['s_up'], 'L0_ffn_wq_down': _L0_ffn_in['wq_down'], 'L0_ffn_s_down': _L0_ffn_in['s_down'], 'L1_attn_ln_w': _L1_attn_in['ln_w'], 'L1_attn_ln_b': _L1_attn_in['ln_b'], 'L1_attn_W_in': _L1_attn_in['W_in'], 'L1_attn_W_out': _L1_attn_in['W_out'], 'L1_ffn_W_r': _L1_ffn_in['W_r'], 'L1_ffn_b_r': _L1_ffn_in['b_r'], 'L1_ffn_W1': _L1_ffn_in['W1'], 'L1_ffn_b1': _L1_ffn_in['b1'], 'L1_ffn_W2': _L1_ffn_in['W2'], 'L1_ffn_b2': _L1_ffn_in['b2'], 'L1_ffn_position_ids': _L1_ffn_in['position_ids'], 'L1_ffn_cache_position': _L1_ffn_in['cache_position']}
    _x0 = _d['L0_attn_x']
    _d['L0_attn_x'] = jax.random.normal(jax.random.fold_in(jax.random.key(seed), 1), (2, 1024, 256), dtype=_x0.dtype)
    del _x0
    return _d

def reference(L0_attn_x, L0_attn_w_qkv, L0_attn_w_out, L0_attn_q_norm_w, L0_attn_k_norm_w, L0_ffn_wq_gate, L0_ffn_s_gate, L0_ffn_wq_up, L0_ffn_s_up, L0_ffn_wq_down, L0_ffn_s_down, L1_attn_ln_w, L1_attn_ln_b, L1_attn_W_in, L1_attn_W_out, L1_ffn_W_r, L1_ffn_b_r, L1_ffn_W1, L1_ffn_b1, L1_ffn_W2, L1_ffn_b2, L1_ffn_position_ids, L1_ffn_cache_position):

    def _L0_attn_ref(x, w_qkv, w_out, q_norm_w, k_norm_w):
        import jax, jax.numpy as jnp
        import numpy as np
        N_HEADS = 32
        N_KV_HEADS = 8
        HEAD_DIM = 64
        D_MODEL = 256
        SLIDING_WINDOW = 64
        ROPE_THETA = 10000.0
        PAST_LENGTH = 0
        EPS = 1e-06

        def _rms_norm(x, w):
            xf = x.astype(jnp.float32)
            rms = jax.lax.rsqrt(jnp.mean(xf * xf, axis=-1, keepdims=True) + EPS)
            return (xf * rms).astype(x.dtype) * w

        def _rope(q, k, past_length):
            s, d = (q.shape[2], q.shape[3])
            inv_freq = 1.0 / ROPE_THETA ** (jnp.arange(0, d, 2, dtype=jnp.float32) / d)
            pos = jnp.arange(s, dtype=jnp.float32) + past_length
            ang = pos[:, None] * inv_freq[None, :]
            emb = jnp.concatenate([ang, ang], axis=-1)
            cos, sin = (jnp.cos(emb), jnp.sin(emb))

            def rot_half(x):
                x1, x2 = jnp.split(x, 2, axis=-1)
                return jnp.concatenate([-x2, x1], axis=-1)
            q = q * cos + rot_half(q) * sin
            k = k * cos + rot_half(k) * sin
            return (q, k)

        def _sliding_mask(seq_len, total_len, past_length):
            q_idx = jnp.arange(seq_len)[:, None]
            k_idx = jnp.arange(total_len)[None, :]
            causal = q_idx + past_length >= k_idx
            window = q_idx + past_length - k_idx < SLIDING_WINDOW
            keep = causal & window
            return jnp.where(keep, 0.0, -jnp.inf).astype(jnp.float32)[None, None]
        b, s, _ = x.shape
        n_rep = N_HEADS // N_KV_HEADS
        q_size = N_HEADS * HEAD_DIM
        kv_size = N_KV_HEADS * HEAD_DIM
        qkv = jnp.einsum('bsd,od->bso', x, w_qkv)
        q, k, v = jnp.split(qkv, [q_size, q_size + kv_size], axis=-1)
        q = q.reshape(b, s, N_HEADS, HEAD_DIM).transpose(0, 2, 1, 3)
        k = k.reshape(b, s, N_KV_HEADS, HEAD_DIM).transpose(0, 2, 1, 3)
        v = v.reshape(b, s, N_KV_HEADS, HEAD_DIM).transpose(0, 2, 1, 3)
        q = _rms_norm(q, q_norm_w)
        k = _rms_norm(k, k_norm_w)
        q, k = _rope(q, k, PAST_LENGTH)
        k_rep = jnp.repeat(k, n_rep, axis=1)
        v_rep = jnp.repeat(v, n_rep, axis=1)
        scale = HEAD_DIM ** (-0.5)
        scores = jnp.einsum('bhqd,bhkd->bhqk', q, k_rep) * scale
        scores = scores + _sliding_mask(s, s, PAST_LENGTH)
        probs = jax.nn.softmax(scores, axis=-1)
        attn = jnp.einsum('bhqk,bhkd->bhqd', probs, v_rep)
        attn = attn.transpose(0, 2, 1, 3).reshape(b, s, q_size)
        return jnp.einsum('bso,do->bsd', attn, w_out)

    def _L0_ffn_ref(x, wq_gate, s_gate, wq_up, s_up, wq_down, s_down):
        import jax, jax.numpy as jnp
        import numpy as np
        DIM = 256
        HID = 704
        ZERO_POINT = 128.0

        def _qlinear(x, wq, scale):
            W = (wq.astype(jnp.float32) - ZERO_POINT) * scale[:, None]
            return jnp.einsum('bsd,hd->bsh', x, W)
        gate = _qlinear(x, wq_gate, s_gate)
        gate = jax.nn.silu(gate)
        up = _qlinear(x, wq_up, s_up)
        return _qlinear(gate * up, wq_down, s_down)

    def _L1_attn_ref(X, ln_w, ln_b, W_in, W_out):
        import jax, jax.numpy as jnp
        import numpy as np
        NUM_HEADS = 16
        LN_EPS = 1e-05

        def _rope(x):
            S, D = (x.shape[-2], x.shape[-1])
            rot = D // 2
            inv_freq = 1.0 / 10000.0 ** (jnp.arange(0, rot, 2, dtype=jnp.float32) / rot)
            ang = jnp.arange(S, dtype=jnp.float32)[:, None] * inv_freq[None, :]
            ang = jnp.repeat(ang, 2, axis=-1)
            cos, sin = (jnp.cos(ang), jnp.sin(ang))
            xr, xp = (x[..., :rot], x[..., rot:])
            x1, x2 = (xr[..., 0::2], xr[..., 1::2])
            rot_half = jnp.stack((-x2, x1), axis=-1).reshape(xr.shape)
            xr = xr * cos + rot_half * sin
            return jnp.concatenate([xr, xp], axis=-1)
        B, S, D = X.shape
        H = NUM_HEADS
        Dh = D // H
        mu = jnp.mean(X, axis=-1, keepdims=True)
        var = jnp.mean(jnp.square(X - mu), axis=-1, keepdims=True)
        Xn = (X - mu) * jax.lax.rsqrt(var + LN_EPS) * ln_w + ln_b
        qkv = jnp.einsum('bsd,df->bsf', Xn, W_in)
        Q, K, V = jnp.split(qkv, 3, axis=-1)
        Q = Q.reshape(B, S, H, Dh).transpose(0, 2, 1, 3)
        K = K.reshape(B, S, H, Dh).transpose(0, 2, 1, 3)
        V = V.reshape(B, S, H, Dh).transpose(0, 2, 1, 3)
        Q, K = (_rope(Q), _rope(K))
        scores = jnp.einsum('bhqd,bhkd->bhqk', Q, K) / jnp.sqrt(jnp.float32(Dh))
        probs = jax.nn.softmax(scores, axis=-1)
        ctx = jnp.einsum('bhqk,bhkd->bhqd', probs, V)
        ctx = ctx.transpose(0, 2, 1, 3).reshape(B, S, D)
        out = jnp.einsum('bsd,df->bsf', ctx, W_out)
        return out + X

    def _L1_ffn_ref(x, W_r, b_r, W1, b1, W2, b2, position_ids, cache_position):
        import jax, jax.numpy as jnp
        import numpy as np
        B, S, D = (4, 512, 256)
        DFF = 4 * D
        CAPACITY = 0.125
        K = int(CAPACITY * S)
        b, s, d = x.shape
        weights = jnp.einsum('bsd,do->bso', x, W_r).squeeze(-1) + b_r
        topk_vals, topk_idx = jax.lax.top_k(weights, K)
        threshold = topk_vals[:, -1]
        sel_mask = weights > threshold[:, None]
        xg = jnp.take_along_axis(x, topk_idx[..., None], axis=1)
        h = jax.nn.gelu(jnp.einsum('bkd,df->bkf', xg, W1) + b1)
        blk = jnp.einsum('bkf,fd->bkd', h, W2) + b2
        gate = (topk_vals > threshold[:, None]).astype(x.dtype)
        wg = jnp.take_along_axis(weights, topk_idx, axis=1)
        vals = blk * (wg * gate)[..., None]
        bidx = jnp.arange(b)[:, None]
        processed = jnp.zeros_like(x).at[bidx, topk_idx].add(vals)
        return processed + x * (~sel_mask)[..., None].astype(x.dtype)
    x = L0_attn_x
    xn = _layernorm(x, axis=-1)
    x = x + _L0_attn_ref(xn, L0_attn_w_qkv, L0_attn_w_out, L0_attn_q_norm_w, L0_attn_k_norm_w) + _L0_ffn_ref(xn, L0_ffn_wq_gate, L0_ffn_s_gate, L0_ffn_wq_up, L0_ffn_s_up, L0_ffn_wq_down, L0_ffn_s_down)
    xn = _layernorm(x, axis=-1)
    x = x + _L1_attn_ref(xn, L1_attn_ln_w, L1_attn_ln_b, L1_attn_W_in, L1_attn_W_out) + _L1_ffn_ref(xn, L1_ffn_W_r, L1_ffn_b_r, L1_ffn_W1, L1_ffn_b1, L1_ffn_W2, L1_ffn_b2, L1_ffn_position_ids, L1_ffn_cache_position)
    return x

_drawn_inputs = setup_inputs


def setup_inputs(seed=0):
    import zlib

    import numpy as np

    out = dict(_drawn_inputs(seed))
    spreads = {'L0_attn_q_norm_w': (1.0, 0.2),
     'L0_attn_k_norm_w': (1.0, 0.2),
     'L1_attn_ln_w': (1.0, 0.6),
     'L1_attn_ln_b': (0.0, 0.8),
     'L1_ffn_b1': (0.0, 2.0),
     'L1_ffn_b2': (0.0, 2.0)}
    factors = {'L0_ffn_s_gate': 8.0,
     'L0_ffn_s_up': 8.0,
     'L0_ffn_s_down': 4.649,
     'L1_attn_W_in': 8.0,
     'L1_attn_W_out': 8.0}
    for name, (base, spread) in spreads.items():
        noise = np.random.default_rng([zlib.crc32(name.encode()), seed]).standard_normal(out[name].shape)
        drawn = base * np.exp(spread * noise) if base else spread * noise
        out[name] = jnp.asarray(drawn.astype(out[name].dtype))
    for name, factor in factors.items():
        out[name] = (out[name] * factor).astype(out[name].dtype)
    return out
```

```python
from contextlib import ExitStack

import concourse.bass as bass
from concourse import mybir

F32 = mybir.dt.float32
F16 = mybir.dt.float16
BF16 = mybir.dt.bfloat16
I32 = mybir.dt.int32
ALU = mybir.AluOpType
ACT = mybir.ActivationFunctionType
AX = mybir.AxisListType

P = 128
B, S, D = 2, 1024, 256
NT = B * S // P
NI = S // P
KC = D // P
HQ, HKV, HD, WIN = 32, 8, 64, 64
G = HKV
REP = HQ // HKV
NH = REP + 1
CW = (REP + 2) * HD
RMS_EPS, LN_EPS = 1e-6, 1e-5
WS = 64.0
HID = 704
HC = HID // G
HP = 96
ZERO_POINT = 128.0
MASKED = -60000.0
H1, D1, ROT1 = 16, 16, 8
W1C = 3 * D // 2
CT = 2 * HD + 2 * ROT1

ITEMS = B * H1
LAST = ITEMS + 3
CGR = 32
NST = 6
ST = NST * D1
DFF = 4 * D
CAP = S // 16
NEVER = -3.0e38
FAR = 1000.0

LAG_A = 8
LAG_N = 9
LAG_T = 10
LAG_S = 11
LAG_V = 13
LAG_O = 14
LAG_W = 15


class Tile:

    def __init__(self, m, c):
        self.m, self.c = m, c
        self.par = c % 2
        self.n = c if m is None else m * 2 + c
        self.i = c // 2 if m is None else m + c // 2
        self.ok = m is not None or 0 <= c < NT

    def back(self, k):
        return Tile(self.m, self.c - k)

    def at(self, lag, g):
        s = g - lag
        return self.back(-(s // G)), s % G


def done(t, g, back=0):
    return t.n * G + (g + 1 - back)


def wait(eng, sem, count):
    if isinstance(count, int) and count <= 0:
        return
    eng.wait_ge(sem, count)


def first(eng, address):
    return address if isinstance(address, int) else eng.snap(address)


def steps(eng, slot):
    for c in range(6):
        for g in range(G):
            slot(Tile(None, c), g)
    with eng.Fori(0, (NT - 6) // 2) as m:
        for c in (6, 7):
            for g in range(G):
                slot(Tile(m, c), g)
    for c in range(NT, NT + 5):
        for g in range(G):
            slot(Tile(None, c), g)


def build(nc, x, w_qkv, w_o, q_w, k_w, w_gate, w_up, s_gate, s_up, w_down, s_down, ln_w, ln_b, w_in, w_r,
          pos_table, masks, eye, w_out1, b_r, w1, b1, w2, b2, before, fold, slots, out):
    with ExitStack() as ctx:
        idf = ctx.enter_context(nc.sbuf_tensor("idf", [P, P], F32))
        xn2_all = ctx.enter_context(nc.sbuf_tensor("xn2_all", [P, NT, D + 1], F32))
        qkv1_all = ctx.enter_context(nc.sbuf_tensor("qkv1_all", [P, B * H1 * NI * 3 * D1], F32))
        layer0(nc, ctx, idf, xn2_all, qkv1_all, x, w_qkv, w_o, q_w, k_w, w_gate, w_up, s_gate, s_up, w_down, s_down,
               ln_w, ln_b, w_in, w_r, pos_table, masks, eye, out)
        layer1(nc, idf, xn2_all, qkv1_all, w_out1, b_r, w1, b1, w2, b2, before, fold, slots, out)


def layer0(nc, whole, idf, xn2_all, qkv1_all, x, w_qkv, w_o, q_w, k_w, w_gate, w_up, s_gate, s_up, w_down, s_down,
           ln_w, ln_b, w_in, w_r, pos_table, masks, eye, out):
    with ExitStack() as ctx:
        def sb(name, shape, dt=F32):
            return ctx.enter_context(nc.sbuf_tensor(name, shape, dt))

        def ps(name, shape, dt=F32):
            return ctx.enter_context(nc.psum_tensor(name, shape, dt))

        def sem(name):
            return whole.enter_context(nc.semaphore(name))

        x1_dram = out

        wq_hi = sb("wq_hi", [P, KC, G, CW], F16)
        wq_lo = sb("wq_lo", [P, KC, G, CW], F16)
        gu_hi = sb("gu_hi", [P, KC, G, 2, HP], F16)
        gu_lo = sb("gu_lo", [P, KC, G, 2, HP], F16)
        wd = sb("wd", [HP, G, D])
        wo = sb("wo", [P, G, 2, D])
        win = sb("win", [P, KC, 3 * D])
        w5c = sb("w5c", [P, NH, HD])
        w5s = sb("w5s", [P, NH, HD])
        sgh = sb("sgh", [HC, G])
        sup = sb("sup", [HC, G])
        sgu = sb("sgu", [HP, G])
        sgp = sb("sgp", [HP, G])
        lnw = sb("lnw", [P, D])
        lnb = sb("lnb", [P, D])
        wr = sb("wr", [P, D])
        idh = sb("idh", [P, P], F16)
        half_neg = sb("half_neg", [P, 8])
        neg_bound = sb("neg_bound", [P, 1])
        wmax = sb("wmax", [P, 2])
        mask_all = sb("mask_all", [P, 2, WIN], F16)
        n_qk = B * H1 * NI * 2 * D1
        qk1_all = qkv1_all[:, 0:n_qk].rearrange("p (b h i e) -> p b h i e", b=B, h=H1, i=NI)
        vv1_all = qkv1_all[:, n_qk:].rearrange("p (b h i e) -> p b h i e", b=B, h=H1, i=NI)
        xa = sb("xa", [P, 2, D])
        xc = sb("xc", [P, 2, D])
        tab = sb("tab", [P, 2, 2 * HD])
        tabr = sb("tabr", [P, 2, 2 * ROT1])
        tcw = sb("tcw", [P, 2, 2, NH, HD])
        st1 = sb("st1", [P, 2, 6])
        mv1 = sb("mv1", [P, 2, 2])
        ve1 = sb("ve1", [P, 2, 1])
        rs1 = sb("rs1", [P, 2, 1])
        xn = sb("xn", [P, D])
        xh = sb("xh", [P, 2, KC, P], F16)
        xl = sb("xl", [P, 2, KC, P], F16)
        sq = sb("sq", [P, NH, HD])
        ss = sb("ss", [P, 2, NH])
        ve = sb("ve", [P, 2, NH])
        rm = sb("rm", [P, 2, NH])
        t1 = sb("t1", [P, 2, NH, HD])
        t2 = sb("t2", [P, NH, HD])
        nat = sb("nat", [P, 2, REP + 2, P], F16)
        qt = sb("qt", [P, 2, REP, P], F16)
        kts = sb("kts", [P, 2, 2, G, WIN + P], F16)
        v0 = sb("v0", [P, 2, G, HD + 1])
        v1 = sb("v1", [P, 2, G, HD + 1])
        pm = sb("probs", [P, 2, 2, REP, WIN])
        mk = sb("mk", [P, 2, 2, WIN], F16)
        th = sb("th", [HP, 2, P])
        fa = sb("fa", [HP, 2, P])
        ht = sb("ht", [HP, G, P])
        rc = sb("rc", [P, 2, 4])
        an = sb("an", [P, 2, 2, 2, HD])
        ats = sb("ats", [P, 2, 2, 2, WIN])
        st2 = sb("st2", [P, 2, 6])
        mv2 = sb("mv2", [P, 2, 2])
        ve2 = sb("ve2", [P, 2, 1])
        rs2 = sb("rs2", [P, 2, 1])
        xs = sb("xs", [P, 2, D + 1])
        st3 = sb("st3", [P, 2, 6])
        mv3 = sb("mv3", [P, 2, 2])
        ve3 = sb("ve3", [P, 2, 1])
        rs3 = sb("rs3", [P, 2, 1])
        xl1 = sb("xl1", [P, D])
        xt1 = sb("xt1", [P, KC, P])
        qs = sb("qs", [P, 3 * D])
        r1 = sb("r1", [P, 2 * H1, ROT1])
        r2 = sb("r2", [P, 2 * H1, ROT1])

        qk = [ps(f"qk{j}", [P, 512]) for j in range(2)]
        tr = ps("tr", [P, 8, P], F16)
        sc = ps("sc", [P, 2, REP, WIN])
        pv = ps("pv", [P, 512])
        pvv = pv[:, 0:4 * (HD + 1)].rearrange("p (a d) -> p a d", a=4)
        at = ps("at", [P, 512])
        atv = at[:, 0:256].rearrange("p (h a q) -> p h a q", h=2, a=2)
        ob = ps("ob", [P, 512])
        ff = ps("ff", [P, 512])
        ffv = ff[:, 0:2 * P].rearrange("p (j t) -> p j t", j=2)

        ld = [sem(f"ld{j}") for j in range(6)]
        names = ("pe_A pe_F pe_T pe_S pe_V pe_O pe_W pe_lnt pe_xat pe_l1 "
                 "act_sq act_A act_hi act_th act_kt act_exp act_at act_xh act_xat act_l1 "
                 "dve_A dve_ss dve_ve dve_kc dve_dup dve_a dve_h dve_qt dve_rc dve_an dve_xl "
                 "dve_b1 dve_g1 dve_v1 dve_xn dve_mk dve_x1 dve_b2 dve_g2 dve_v2 dve_xs dve_wr dve_b3 dve_g3 dve_v3 "
                 "dve_xa "
                 "pool_rm pool_u pool_v pool_lo pool_rs1 pool_rs2 pool_rs3 pool_tcw pool_lw pool_xa "
                 "pool_r1 pool_r2 pool_rope set_act set_dve set_pool").split()
        s_ = {n: sem(n) for n in names}
        xa_ld = [sem(f"xa_ld{j}") for j in range(2)]
        xc_ld = [sem(f"xc_ld{j}") for j in range(2)]
        tab_ld = [sem(f"tab_ld{j}") for j in range(2)]
        tabr_ld = [sem(f"tabr_ld{j}") for j in range(2)]
        vca = [sem(f"v_carried{j}") for j in range(G)]
        vnw = [sem(f"v_placed{j}") for j in range(G)]
        x1_st = [sem(f"x1_stored{j}") for j in range(2)]
        xs_st = [sem(f"xs_stored{j}") for j in range(2)]
        qs_st = sem("qk_stored")
        vs_st = sem("v_stored")

        stage = qkv1_all[:, :]
        wq_f = stage[:, 0:KC * G * CW].rearrange("p (k g c) -> p k g c", k=KC, g=G)
        o1 = KC * G * CW
        n_gu = KC * G * HC
        gu_i = [stage[:, o1 + j * n_gu:o1 + (j + 1) * n_gu].bitcast(I32).rearrange("p (k g c) -> p k g c", k=KC, g=G)
                for j in range(2)]
        stage2 = xn2_all[:, :, :].rearrange("p n d -> p (n d)")
        gu_f = [stage2[:, j * n_gu:(j + 1) * n_gu].rearrange("p (k g c) -> p k g c", k=KC, g=G) for j in range(2)]
        o2 = o1 + 2 * n_gu
        wd_i = stage[0:HC, o2:o2 + G * D].bitcast(I32).rearrange("p (g d) -> p g d", g=G)
        sd_b = stage[0:HC, o2 + G * D:o2 + G * D + D]

        EXTRA = qk[1]

        def BANK(k):
            return qk[k % 2 if k < 4 else 0]

        block = ctx.enter_context(nc.Block())

        @block.sync
        def _(sp):
            sp.dma_start(wq_f, w_qkv).then_inc(ld[0], 16)
            sp.dma_start(idf[:, :], eye).then_inc(ld[1], 16)
            for h in range(NH):
                w = k_w if h == REP else q_w
                sp.dma_start(w5c[:, h, :], w.broadcast_to([P, HD])).then_inc(ld[2], 16)
                for half in range(2):
                    sp.dma_start(w5s[:, h, 32 * half:32 * half + 32],
                                 w[:, 32 - 32 * half:64 - 32 * half].broadcast_to([P, 32])).then_inc(ld[2], 16)
            sp.dma_start(mk[:, 0, :, :], masks[0]).then_inc(ld[3], 16)
            sp.dma_start(mk[:, 1, :, :], masks[0]).then_inc(ld[3], 16)
            sp.dma_start(mask_all[:, :, :], masks[1]).then_inc(ld[3], 16)
            sp.dma_start(gu_i[0], w_gate).then_inc(ld[4], 16)
            sp.dma_start(gu_i[1], w_up).then_inc(ld[4], 16)
            sp.dma_start(sgh[:, :], s_gate).then_inc(ld[4], 16)
            sp.dma_start(sup[:, :], s_up).then_inc(ld[4], 16)
            sp.dma_start(wd_i, w_down).then_inc(ld[4], 16)
            sp.dma_start(sd_b, s_down.broadcast_to([HC, D])).then_inc(ld[4], 16)
            sp.dma_start(wo[:, :, :, :], w_o).then_inc(ld[5], 16)
            sp.dma_start(win[:, :, :], w_in).then_inc(ld[5], 16)
            sp.dma_start(lnw[:, :], ln_w.broadcast_to([P, D])).then_inc(ld[5], 16)
            sp.dma_start(lnb[:, :], ln_b.broadcast_to([P, D])).then_inc(ld[5], 16)
            sp.dma_start(wr[:, :], w_r.broadcast_to([P, D])).then_inc(ld[5], 16)
            def slot(T, g):
                if g == 0 and T.ok:
                    row = first(sp, T.n * P)
                    wait(sp, s_["dve_xn"], T.n - 1)
                    sp.dma_start(xa[:, T.par, :], x[bass.ds(row, P), :]).then_inc(xa_ld[T.par], 16)
                t = T
                if t.ok:
                    if t.m is not None or t.c >= 2:
                        wait(sp, s_["pe_V"], done(t.back(2), g))
                        sp.dma_start(v0[0:WIN, t.par, g, :], v1[WIN:P, t.par, g, :]).then_inc(vca[g], 16)
                t, k = T.at(LAG_A, g)
                if t.ok:
                    wait(sp, s_["act_A"], done(t, k))
                    if not T.ok:
                        wait(sp, s_["pe_V"], done(t.back(2), k))
                    sp.dma_start(v0[WIN:P, t.par, k, :], v1[0:WIN, t.par, k, :]).then_inc(vnw[k], 16)
                if g == 1 and T.ok:
                    row = first(sp, T.i * P)
                    wait(sp, s_["pool_tcw"], T.n - 1)
                    sp.dma_start(tab[:, T.par, :], pos_table[bass.ds(row, P), 0:2 * HD]).then_inc(tab_ld[T.par], 16)
                t = T.back(2)
                if g == 1 and t.ok:
                    row = first(sp, t.n * P)
                    wait(sp, s_["dve_xa"], t.n - 1)
                    sp.dma_start(xc[:, t.par, :], x[bass.ds(row, P), :]).then_inc(xc_ld[t.par], 16)
                t = T.back(3)
                if g == 1 and t.ok:
                    row, place, roped = first(sp, t.n * P), first(sp, t.i * P), first(sp, t.n - 1)
                    wait(sp, s_["dve_x1"], t.n + 1)
                    sp.dma_start(x1_dram[bass.ds(row, P), :], xc[:, t.par, :]).then_inc(x1_st[t.par], 16)
                    wait(sp, s_["pool_rope"], roped)
                    sp.dma_start(tabr[:, t.par, :], pos_table[bass.ds(place, P), 2 * HD:CT]).then_inc(tabr_ld[t.par], 16)
                if g == 3 and t.ok:
                    place = first(sp, t.n)
                    if t.m is None and t.c == 0:
                        sp.wait_ge(s_["set_dve"], 1)
                    wait(sp, s_["dve_wr"], t.n + 1)
                    sp.dma_start(xn2_all[:, bass.ds(place, 1), :], xs[:, t.par:t.par + 1, :]).then_inc(xs_st[t.par], 16)
                t = T.back(4)
                if g == 4 and t.ok:
                    place = first(sp, t.i)
                    wait(sp, s_["pool_rope"], t.n + 1)
                    sp.dma_start(qk1_all[:, t.par, :, bass.ds(place, 1), :],
                                 qs[:, 0:2 * D].rearrange("p (h o e) -> p h o e", h=H1, o=1)).then_inc(qs_st, 16)
                    sp.dma_start(vv1_all[:, t.par, :, bass.ds(place, 1), :],
                                 qs[:, 2 * D:3 * D].rearrange("p (h o e) -> p h o e", h=H1, o=1)).then_inc(vs_st, 16)

            steps(sp, slot)
            for j in range(2):
                sp.wait_ge(xs_st[j], 16 * (NT // 2))
                sp.wait_ge(x1_st[j], 16 * (NT // 2))
            sp.wait_ge(qs_st, 16 * NT)
            sp.wait_ge(vs_st, 16 * NT)
            sp.wait_ge(s_["pool_rope"], NT)

        @block.scalar
        def _(act):
            def ev(dst, src, scale=1.0):
                return act.activation(dst, src, ACT.Copy, scale=scale)

            act.wait_ge(ld[0], 16)
            ev(wq_hi[:, :, :, :], wq_f, WS).then_inc(s_["set_act"], 1)

            def slot(T, g):
                t, k = T.at(LAG_A, g)
                b = k % 2
                if t.ok:
                    act.wait_ge(s_["pe_A"], done(t, k))
                    wait(act, s_["dve_ss"], done(t, k, 1))
                    act.activation(sq[:, :, :], BANK(k)[:, 0:NH * HD], ACT.Square,
                                   scale=1.0 / 8).then_inc(s_["act_sq"], 1)
                    if t.m is not None or t.c >= 2:
                        act.wait_ge(vca[k], (t.n - 1) * 16)
                        act.wait_ge(vnw[k], (t.n - 1) * 16)
                    else:
                        act.wait_ge(s_["set_pool"], 1)
                    ev(v1[:, t.par, k, 0:HD], BANK(k)[:, NH * HD:CW], 1.0 / WS).then_inc(s_["act_A"], 1)
                t, k = T.at(LAG_N, g)
                b = k % 2
                if t.ok:
                    act.wait_ge(s_["pool_v"], done(t, k))
                    wait(act, s_["pe_T"], done(t, k, 2))
                    ev(nat[:, b, 0:NH, 0:HD], t1[:, b, :, :]).then_inc(s_["act_hi"], 1)
                t, k = T.at(LAG_A, g)
                b = k % 2
                if t.ok:
                    act.wait_ge(s_["pe_F"], done(t, k))
                    wait(act, s_["dve_a"], done(t, k, 2))
                    if k == 0 and not (t.m is not None or t.c > 0):
                        act.wait_ge(s_["set_dve"], 1)
                    act.activation(th[:, b, :], ffv[0:HP, 0, :], ACT.Tanh,
                                   scale=sgp[:, k:k + 1]).then_inc(s_["act_th"], 1)
                t, k = T.at(LAG_T, g)
                if t.ok:
                    act.wait_ge(s_["pe_T"], done(t, k))
                    if t.m is not None or t.c >= 2:
                        act.wait_ge(s_["dve_kc"], done(t.back(2), k))
                    else:
                        act.wait_ge(s_["set_pool"], 1)
                    ev(kts[:, t.par, :, k, WIN:WIN + P], tr[:, REP:REP + 2, :]).then_inc(s_["act_kt"], 1)
                t, k = T.at(LAG_S, g)
                b = k % 2
                if t.ok:
                    act.wait_ge(s_["pe_S"], done(t, k))
                    wait(act, s_["pe_V"], done(t, k, 2))
                    act.activation(pm[:, b, :, :, :], sc[:, :, :, :], ACT.Exp, bias=neg_bound[:, 0:1],
                                   scale=HD ** -0.5).then_inc(s_["act_exp"], 1)
                t, k = T.at(LAG_O, g)
                b = k % 2
                if t.ok:
                    act.wait_ge(s_["pe_O"], done(t, k))
                    wait(act, s_["pe_W"], done(t, k, 2))
                    ev(ats[:, b, :, :, :].rearrange("p a h q -> p h a q"), atv).then_inc(s_["act_at"], 1)
                if g == 5 and T.ok:
                    act.wait_ge(s_["pe_lnt"], T.n + 1)
                    wait(act, s_["pe_A"], done(T.back(2), G - 1))
                    wait(act, s_["pe_F"], done(T.back(2), G - 1))
                    ev(xh[:, T.par, :, :], EXTRA[:, 0:D].rearrange("p (k t) -> p k t", k=KC)).then_inc(s_["act_xh"], 1)
                t = T.back(3)
                if g == 5 and t.ok:
                    act.wait_ge(s_["pe_xat"], t.n + 1)
                    ev(xt1[:, :, :], EXTRA[:, 0:D].rearrange("p (k t) -> p k t", k=KC)).then_inc(s_["act_xat"], 1)
                if g in (6, 7) and t.ok:
                    h = g - 6
                    act.wait_ge(s_["pe_l1"], t.n * 2 + h + 1)
                    if h == 0:
                        wait(act, qs_st, t.n * 16)
                        wait(act, vs_st, t.n * 16)
                    ev(qs[:, h * W1C:(h + 1) * W1C], EXTRA[:, 0:W1C]).then_inc(s_["act_l1"], 1)

            steps(act, slot)

        @block.vector
        def _(dve):
            chain = sem("dve_chain")
            n_chain = [0]

            def link(ins):
                n_chain[0] += 1
                ins.then_inc(chain, 1)
                dve.wait_ge(chain, n_chain[0])

            dve.memset(half_neg[:, :], -0.5)
            link(dve.memset(wd[:, :, :], 0.0))
            link(dve.memset(sgu[:, :], 0.0))
            link(dve.memset(sgp[:, :], 0.0))
            link(dve.memset(gu_hi[:, :, :, :, :], 0.0))
            link(dve.memset(gu_lo[:, :, :, :, :], 0.0))
            dve.wait_ge(ld[1], 16)
            link(dve.tensor_copy(idh[:, :], idf[:, :]))
            dve.wait_ge(ld[2], 16 * 3 * NH)
            dve.tensor_reduce(wmax[:, 0:1], w5c[:, 0, :], AX.X, ALU.max, apply_absolute_value=True)
            link(dve.tensor_reduce(wmax[:, 1:2], w5c[:, REP, :], AX.X, ALU.max, apply_absolute_value=True))
            link(dve.tensor_scalar(neg_bound[:, :], wmax[:, 0:1], wmax[:, 1:2], -float(HD) * HD ** -0.5,
                                   ALU.mult, ALU.mult))
            dve.wait_ge(s_["set_act"], 1)
            link(dve.scalar_tensor_tensor(wq_lo[:, :, :, :], wq_f, WS, wq_hi[:, :, :, :], ALU.mult, ALU.subtract))
            dve.wait_ge(ld[4], 16 * 6)
            for j in range(2):
                link(dve.tensor_scalar(gu_f[j], gu_i[j], -ZERO_POINT, None, ALU.add))
                link(dve.tensor_copy(gu_hi[:, :, :, j, 0:HC], gu_f[j]))
                link(dve.tensor_tensor(gu_lo[:, :, :, j, 0:HC], gu_f[j], gu_hi[:, :, :, j, 0:HC], ALU.subtract))
            link(dve.tensor_scalar(sgp[0:HC, :], sgh[:, :], 0.5, None, ALU.mult))
            link(dve.tensor_tensor(sgu[0:HC, :], sgp[0:HC, :], sup[:, :], ALU.mult))
            link(dve.tensor_scalar(wd[0:HC, :, :], wd_i, -ZERO_POINT, None, ALU.add))
            dve.tensor_tensor(wd[0:HC, :, :], wd[0:HC, :, :], sd_b.unsqueeze(1).broadcast_to([HC, G, D]),
                              ALU.mult).then_inc(s_["set_dve"], 1)
            dve.wait_ge(ld[3], 48)
            dve.wait_ge(ld[5], 16 * 5)

            def norm_stats(st, mv, v, src, par, b, gg, vv, n):
                dve.bn_stats(st[:, par, :], src).then_inc(s_[b], 1)
                dve.wait_ge(s_[b], n + 1)
                dve.memset(v[:, par, :], LN_EPS)
                dve.bn_aggr(mv[:, par, :], st[:, par, :]).then_inc(s_[gg], 1)
                dve.wait_ge(s_[gg], n + 1)
                dve.tensor_tensor(v[:, par, :], v[:, par, :], mv[:, par, 1:2], ALU.add).then_inc(s_[vv], 1)

            def slot(T, g):
                t, k = T.at(LAG_A, g)
                b = k % 2
                if t.ok:
                    if k == 0:
                        dve.wait_ge(s_["pool_tcw"], t.n + 1)
                    dve.wait_ge(s_["pe_A"], done(t, k))
                    wait(dve, s_["pool_lo"], done(t, k, 2))
                    wait(dve, s_["pool_u"], done(t, k, 1))
                    heads = BANK(k)[:, 0:NH * HD].rearrange("p (h d) -> p h d", h=NH)
                    swapped = BANK(k)[:, 0:NH * HD].rearrange("p (h a d) -> p h a d", h=NH, a=2)[:, :, ::-1, :]
                    dve.wait_ge(s_["act_A"], done(t, k))
                    dve.tensor_tensor(t1[:, b, :, :], heads, tcw[:, t.par, 0, :, :], ALU.mult)
                    dve.tensor_tensor(t2[:, :, :].rearrange("p h (a d) -> p h a d", a=2), swapped,
                                      tcw[:, t.par, 1, :, :].rearrange("p h (a d) -> p h a d", a=2),
                                      ALU.mult).then_inc(s_["dve_A"], 1)
                    dve.wait_ge(s_["act_sq"], done(t, k))
                    dve.tensor_reduce(ss[:, b, :], sq[:, :, :], AX.X, ALU.add).then_inc(s_["dve_ss"], 1)
                    dve.wait_ge(s_["dve_ss"], done(t, k))
                    wait(dve, s_["pool_rm"], done(t, k, 2))
                    dve.tensor_scalar(ve[:, b, :], ss[:, b, :], WS * WS * RMS_EPS, None, ALU.add).then_inc(s_["dve_ve"], 1)
                t, k = T.at(LAG_T, g)
                if t.ok and (t.m is not None or t.c >= 2):
                    dve.wait_ge(s_["pe_S"], done(t.back(2), k))
                    dve.tensor_copy(kts[:, t.par, :, k, 0:WIN], kts[:, t.par, :, k, P:P + WIN]).then_inc(s_["dve_kc"], 1)
                t, k = T.at(LAG_A, g)
                b = k % 2
                if t.ok:
                    dve.wait_ge(s_["act_th"], done(t, k))
                    wait(dve, s_["dve_h"], done(t, k, 2))
                    dve.scalar_tensor_tensor(fa[:, b, :], th[:, b, :], 1.0, ffv[0:HP, 0, :], ALU.add,
                                             ALU.mult).then_inc(s_["dve_a"], 1)
                    dve.wait_ge(s_["dve_a"], done(t, k))
                    wait(dve, s_["pe_W"], done(t.back(1), k))
                    dve.scalar_tensor_tensor(ht[:, k, :], ffv[0:HP, 1, :], sgu[:, k:k + 1], fa[:, b, :], ALU.mult,
                                             ALU.mult).then_inc(s_["dve_h"], 1)
                t, k = T.at(LAG_N, g)
                b = k % 2
                if t.ok:
                    dve.wait_ge(s_["pool_lo"], done(t, k))
                    dve.tensor_copy(nat[:, b, REP:REP + 2, HD:P], nat[:, b, REP:REP + 2, 0:HD]).then_inc(s_["dve_dup"], 1)
                t, k = T.at(LAG_T, g)
                b = k % 2
                if t.ok:
                    dve.wait_ge(s_["act_kt"], done(t, k))
                    wait(dve, s_["pe_S"], done(t, k, 2))
                    dve.tensor_copy(qt[:, b, :, :], tr[:, 0:REP, :]).then_inc(s_["dve_qt"], 1)
                t, k = T.at(LAG_V, g)
                b = k % 2
                if t.ok:
                    dve.wait_ge(s_["pe_V"], done(t, k))
                    dve.reciprocal(rc[:, b, :], pvv[:, :, HD]).then_inc(s_["dve_rc"], 1)
                    dve.wait_ge(s_["dve_rc"], done(t, k))
                    wait(dve, s_["pe_O"], done(t, k, 2))
                    dve.tensor_tensor(an[:, b, :, :, :].rearrange("p h a d -> p (h a) d"), pvv[:, :, 0:HD],
                                      rc[:, b, :].unsqueeze(2).broadcast_to([P, 4, HD]), ALU.mult).then_inc(s_["dve_an"], 1)
                if g == 1 and T.ok:
                    dve.wait_ge(xa_ld[T.par], T.i * 16 + 16)
                    norm_stats(st1, mv1, ve1, xa[:, T.par, :], T.par, "dve_b1", "dve_g1", "dve_v1", T.n)
                if g == 3 and T.ok:
                    dve.wait_ge(s_["pool_rs1"], T.n + 1)
                    wait(dve, s_["pe_lnt"], T.n)
                    dve.tensor_scalar(xn[:, :], xa[:, T.par, :], mv1[:, T.par, 0:1], rs1[:, T.par, :],
                                      ALU.subtract, ALU.mult).then_inc(s_["dve_xn"], 1)
                if g == 5 and T.ok:
                    dve.wait_ge(s_["act_xh"], T.n + 1)
                    dve.tensor_tensor(xl[:, T.par, :, :], EXTRA[:, 0:D].rearrange("p (k t) -> p k t", k=KC),
                                      xh[:, T.par, :, :], ALU.subtract).then_inc(s_["dve_xl"], 1)
                t = T.back(2)
                if g == 3 and t.ok:
                    dve.wait_ge(s_["pe_S"], done(t, G - 1))
                    dve.tensor_copy(mk[:, t.par, :, :], mask_all[:, :, :]).then_inc(s_["dve_mk"], 1)
                if g == 7 and t.ok:
                    dve.wait_ge(s_["pe_W"], done(t, G - 1))
                    dve.wait_ge(xc_ld[t.par], t.i * 16 + 16)
                    dve.tensor_tensor(xc[:, t.par, :], ob[:, 0:D], xc[:, t.par, :], ALU.add).then_inc(s_["dve_x1"], 1)
                    dve.wait_ge(s_["dve_x1"], t.n + 1)
                    norm_stats(st2, mv2, ve2, xc[:, t.par, :], t.par, "dve_b2", "dve_g2", "dve_v2", t.n)
                t = T.back(3)
                if g == 1 and t.ok:
                    dve.wait_ge(s_["pool_rs2"], t.n + 1)
                    wait(dve, xs_st[t.par], t.i * 16)
                    dve.tensor_scalar(xs[:, t.par, 0:D], xc[:, t.par, :], mv2[:, t.par, 0:1], rs2[:, t.par, :],
                                      ALU.subtract, ALU.mult).then_inc(s_["dve_xs"], 1)
                    dve.wait_ge(s_["dve_xs"], t.n + 1)
                    norm_stats(st3, mv3, ve3, xs[:, t.par, 0:D], t.par, "dve_b3", "dve_g3", "dve_v3", t.n)
                    wait(dve, s_["pe_xat"], t.n)
                    dve.tensor_tensor_reduce(out=xl1[:, :], in0=xs[:, t.par, 0:D], in1=wr[:, :], scale=1.0, scalar=0.0,
                                             op0=ALU.mult, op1=ALU.add,
                                             accum_out=xs[:, t.par, D:D + 1]).then_inc(s_["dve_wr"], 1)
                if g == 3 and t.ok:
                    dve.wait_ge(s_["pool_rs3"], t.n + 1)
                    dve.wait_ge(x1_st[t.par], t.i * 16 + 16)
                    dve.wait_ge(s_["dve_wr"], t.n + 1)
                    dve.tensor_scalar(xl1[:, :], xs[:, t.par, 0:D], mv3[:, t.par, 0:1], rs3[:, t.par, :],
                                      ALU.subtract, ALU.mult).then_inc(s_["dve_xa"], 1)

            steps(dve, slot)

        @block.gpsimd
        def _(pool):
            pool.memset(kts[:, :, :, :, :], 0.0)
            pool.memset(v0[:, :, :, :], 0.0)
            pool.memset(v1[:, :, :, :], 1.0).then_inc(s_["set_pool"], 1)
            pool.wait_ge(ld[2], 16 * 3 * NH)
            pool.wait_ge(ld[3], 48)
            pool.wait_ge(ld[5], 16 * 5)
            pool.wait_ge(s_["set_dve"], 1)

            def rsqrt(dst, src, k=1):
                return pool.tensor_tensor(dst, src, half_neg[:, 0:k], ALU.pow)

            def slot(T, g):
                t, k = T.at(LAG_A, g)
                b = k % 2
                if t.ok:
                    pool.wait_ge(s_["dve_A"], done(t, k))
                    pool.tensor_tensor(t1[:, b, :, :], t1[:, b, :, :], t2[:, :, :], ALU.add).then_inc(s_["pool_u"], 1)
                t, k = T.at(LAG_N, g)
                b = k % 2
                if t.ok:
                    pool.wait_ge(s_["act_hi"], done(t, k))
                    wait(pool, s_["pe_T"], done(t, k, 2))
                    pool.tensor_tensor(nat[:, b, 0:REP, HD:P], t1[:, b, 0:REP, :], nat[:, b, 0:REP, 0:HD], ALU.subtract)
                    pool.tensor_tensor(nat[:, b, REP + 1, 0:HD], t1[:, b, REP, :], nat[:, b, REP, 0:HD],
                                       ALU.subtract).then_inc(s_["pool_lo"], 1)
                t, k = T.at(LAG_A, g)
                b = k % 2
                if t.ok:
                    pool.wait_ge(s_["dve_ve"], done(t, k))
                    rsqrt(rm[:, b, :], ve[:, b, :], NH).then_inc(s_["pool_rm"], 1)
                    pool.wait_ge(s_["pool_rm"], done(t, k))
                    pool.wait_ge(s_["pool_u"], done(t, k))
                    pool.tensor_tensor(t1[:, b, :, :], t1[:, b, :, :], rm[:, b, :].unsqueeze(2).broadcast_to([P, NH, HD]),
                                       ALU.mult).then_inc(s_["pool_v"], 1)
                if g == 2 and T.ok:
                    pool.wait_ge(s_["dve_v1"], T.n + 1)
                    rsqrt(rs1[:, T.par, :], ve1[:, T.par, :]).then_inc(s_["pool_rs1"], 1)
                if g == 6 and T.ok:
                    pool.wait_ge(tab_ld[T.par], T.i * 16 + 16)
                    wait(pool, s_["dve_A"], done(T.back(2), G - 1))
                    for j, w5 in enumerate((w5c, w5s)):
                        ins = pool.tensor_tensor(tcw[:, T.par, j, :, :],
                                                 tab[:, T.par, j * HD:(j + 1) * HD].unsqueeze(1).broadcast_to([P, NH, HD]),
                                                 w5[:, :, :], ALU.mult)
                    ins.then_inc(s_["pool_tcw"], 1)
                t = T.back(3)
                if g == 0 and t.ok:
                    pool.wait_ge(s_["dve_v2"], t.n + 1)
                    rsqrt(rs2[:, t.par, :], ve2[:, t.par, :]).then_inc(s_["pool_rs2"], 1)
                if g == 2 and t.ok:
                    pool.wait_ge(s_["dve_v3"], t.n + 1)
                    rsqrt(rs3[:, t.par, :], ve3[:, t.par, :]).then_inc(s_["pool_rs3"], 1)
                if g == 4 and t.ok:
                    pool.wait_ge(s_["dve_xa"], t.n + 1)
                    pool.tensor_tensor(xl1[:, :], xl1[:, :], lnw[:, :], ALU.mult).then_inc(s_["pool_lw"], 1)
                    pool.wait_ge(s_["pool_lw"], t.n + 1)
                    pool.tensor_tensor(xl1[:, :], xl1[:, :], lnb[:, :], ALU.add).then_inc(s_["pool_xa"], 1)
                t = T.back(4)
                if g == 2 and t.ok:
                    pool.wait_ge(s_["act_l1"], t.n * 2 + 2)
                    wait(pool, s_["pool_rope"], t.n)
                    heads = qs[:, 0:2 * D].rearrange("p (h d) -> p h d", d=D1)[:, :, 0:ROT1]
                    swapped = heads.rearrange("p h (c a) -> p h c a", a=2)[:, :, :, ::-1]
                    pool.wait_ge(tabr_ld[t.par], t.i * 16 + 16)
                    pool.tensor_tensor(r1[:, :, :], heads, tabr[:, t.par, 0:ROT1].unsqueeze(1).broadcast_to(
                        [P, 2 * H1, ROT1]), ALU.mult).then_inc(s_["pool_r1"], 1)
                    pool.tensor_tensor(r2[:, :, :].rearrange("p h (c a) -> p h c a", a=2), swapped,
                                       tabr[:, t.par, ROT1:2 * ROT1].rearrange("p (c a) -> p c a", a=2).unsqueeze(1)
                                       .broadcast_to([P, 2 * H1, ROT1 // 2, 2]), ALU.mult).then_inc(s_["pool_r2"], 1)
                    pool.wait_ge(s_["pool_r1"], t.n + 1)
                    pool.wait_ge(s_["pool_r2"], t.n + 1)
                    pool.tensor_tensor(heads, r1[:, :, :], r2[:, :, :], ALU.add).then_inc(s_["pool_rope"], 1)

            steps(pool, slot)

        @block.tensor
        def _(pe):
            pe.wait_ge(s_["set_dve"], 1)
            pe.wait_ge(ld[1], 16)
            pe.wait_ge(ld[5], 16 * 5)
            pe.wait_ge(s_["set_pool"], 1)

            def slot(T, g):
                t, k = T.at(LAG_A, g)
                if t.ok:
                    if k == 0:
                        pe.wait_ge(s_["dve_xl"], t.n + 1)
                    back = 1 if k >= 5 else 2
                    if k == 0:
                        back = 1
                    if k == 1:
                        back = 2
                        wait(pe, s_["act_l1"], (t.n - 2) * 2)
                    wait(pe, s_["act_A"], done(t, k, back))
                    wait(pe, s_["dve_A"], done(t, k, back))
                    for c in range(KC):
                        for j, (a, w) in enumerate(((xh, wq_hi), (xh, wq_lo), (xl, wq_hi))):
                            ins = pe.matmul(BANK(k)[:, 0:CW], a[:, t.par, c, :], w[:, c, k, :],
                                            start=(c == 0 and j == 0), stop=(c == KC - 1 and j == 2))
                    ins.then_inc(s_["pe_A"], 1)
                    wait(pe, s_["dve_h"], done(t, k, 1))
                    for u in range(2):
                        for c in range(KC):
                            for j, (a, w) in enumerate(((xh, gu_hi), (xh, gu_lo), (xl, gu_hi))):
                                ins = pe.matmul(ffv[0:HP, u, :], w[:, c, k, u, :], a[:, t.par, c, :],
                                                start=(c == 0 and j == 0), stop=(c == KC - 1 and j == 2))
                    ins.then_inc(s_["pe_F"], 1)
                t, k = T.at(LAG_T, g)
                b = k % 2
                if t.ok:
                    pe.wait_ge(s_["dve_dup"], done(t, k))
                    wait(pe, s_["dve_qt"], done(t, k, 1))
                    for j in range(REP + 2):
                        ins = pe.transpose(tr[:, j, :], nat[:, b, j, :], idh[:, :])
                    ins.then_inc(s_["pe_T"], 1)
                t, k = T.at(LAG_S, g)
                b = k % 2
                if t.ok:
                    pe.wait_ge(s_["dve_qt"], done(t, k))
                    wait(pe, s_["act_exp"], done(t, k, 1))
                    if k == 0:
                        wait(pe, s_["dve_mk"], t.n - 1)
                    for h in range(2):
                        pe.matmul(sc[:, h, :, :], idh[:, :], mk[:, t.par, h, :].unsqueeze(1).broadcast_to([P, REP, WIN]),
                                  start=True, stop=False)
                        for j in range(2):
                            ins = pe.matmul(sc[:, h, :, :], kts[:, t.par, j, k, h * WIN:h * WIN + P],
                                            qt[:, b, :, h * WIN:(h + 1) * WIN], start=False, stop=(j == 1))
                    ins.then_inc(s_["pe_S"], 1)
                t, k = T.at(LAG_V, g)
                b = k % 2
                if t.ok:
                    pe.wait_ge(s_["act_exp"], done(t, k))
                    pe.wait_ge(vnw[k], t.n * 16 + 16)
                    if t.m is not None or t.c >= 2:
                        pe.wait_ge(vca[k], (t.n - 1) * 16)
                    wait(pe, s_["dve_an"], done(t, k, 1))
                    for h, v in enumerate((v0, v1)):
                        for a in range(2):
                            ins = pe.matmul(pvv[:, 2 * h + a, :], pm[:, b, h, 2 * a:2 * a + 2, :], v[:, t.par, k, :],
                                            start=True, stop=True)
                    ins.then_inc(s_["pe_V"], 1)
                t, k = T.at(LAG_O, g)
                b = k % 2
                if t.ok:
                    pe.wait_ge(s_["dve_an"], done(t, k))
                    wait(pe, s_["act_at"], done(t, k, 1))
                    for h in range(2):
                        ins = pe.transpose(atv[:, h, :, :], an[:, b, h, :, :], idf[:, :])
                    ins.then_inc(s_["pe_O"], 1)
                t, k = T.at(LAG_W, g)
                b = k % 2
                if t.ok:
                    pe.wait_ge(s_["act_at"], done(t, k))
                    pe.wait_ge(s_["dve_h"], done(t, k))
                    if k == 0:
                        wait(pe, s_["dve_x1"], t.n)
                    for a in range(2):
                        pe.matmul(ob[:, 0:D], ats[:, b, a, :, :], wo[:, k, a, :], start=(k == 0 and a == 0), stop=False)
                    pe.matmul(ob[:, 0:D], ht[:, k, :], wd[:, k, :], start=False, stop=(k == G - 1)).then_inc(s_["pe_W"], 1)
                if g == 4 and T.ok:
                    pe.wait_ge(s_["dve_xn"], T.n + 1)
                    t = T.back(1)
                    wait(pe, s_["act_A"], done(t, 3)) if t.ok else None
                    wait(pe, s_["dve_A"], done(t, 3)) if t.ok else None
                    for c in range(KC):
                        ins = pe.transpose(EXTRA[:, c * P:(c + 1) * P], xn[:, c * P:(c + 1) * P], idf[:, :])
                    ins.then_inc(s_["pe_lnt"], 1)
                t = T.back(3)
                if g == 5 and t.ok:
                    pe.wait_ge(s_["pool_xa"], t.n + 1)
                    if T.ok:
                        pe.wait_ge(s_["dve_xl"], T.n + 1)
                    elif T.back(1).ok:
                        pe.wait_ge(s_["act_A"], done(T.back(1), 3))
                        pe.wait_ge(s_["dve_A"], done(T.back(1), 3))
                    wait(pe, s_["act_l1"], t.n * 2)
                    for c in range(KC):
                        ins = pe.transpose(EXTRA[:, c * P:(c + 1) * P], xl1[:, c * P:(c + 1) * P], idf[:, :])
                    ins.then_inc(s_["pe_xat"], 1)
                if g in (6, 7) and t.ok:
                    h = g - 6
                    if h == 0:
                        pe.wait_ge(s_["act_xat"], t.n + 1)
                    wait(pe, s_["act_l1"], t.n * 2 + h)
                    for c in range(KC):
                        ins = pe.matmul(EXTRA[:, 0:W1C], xt1[:, c, :], win[:, c, h * W1C:(h + 1) * W1C],
                                        start=(c == 0), stop=(c == KC - 1))
                    ins.then_inc(s_["pe_l1"], 1)

            steps(pe, slot)


class Item:

    def __init__(self, m, c):
        self.m, self.c = m, c
        self.par, self.buf = c % 2, c % 4
        self.n = c if m is None else m * 4 + c
        self.half = c // 2 if m is None else m * 2 + c // 2
        self.quarter = c // 4 if m is None else m + c // 4
        self.ok = m is not None or 0 <= c < ITEMS

    def back(self, k):
        return Item(self.m, self.c - k)


def items(eng, unit):
    for c in range(8):
        for u in range(NI):
            unit(Item(None, c), u)
    with eng.Fori(0, (ITEMS - 8) // 4) as m:
        for c in range(8, 12):
            for u in range(NI):
                unit(Item(m, c), u)
    for c in range(ITEMS, ITEMS + 6):
        for u in range(NI):
            unit(Item(None, c), u)


def layer1(nc, idf, xn2_all, qkv1_all, w_out1, b_r, w1, b1, w2, b2, before, fold, slots, out):
    n_qk = ITEMS * NI * 2 * D1
    with ExitStack() as ctx:
        def sb(name, shape, dt=F32):
            return ctx.enter_context(nc.sbuf_tensor("l1_" + name, shape, dt))

        def ps(name, shape, dt=F32):
            return ctx.enter_context(nc.psum_tensor("l1_" + name, shape, dt))

        def sem(name):
            return ctx.enter_context(nc.semaphore("l1_" + name))

        idb = sb("idb", [P, P], BF16)
        ctxn = sb("ctxn", [P, NI, B * D])
        wt1 = sb("wt1", [P, KC, DFF])
        bt1 = sb("bt1", [P, DFF // P])
        wt2 = sb("wt2", [P, DFF // P, D])
        bt2 = sb("bt2", [P, D])
        wou = sb("wou", [P, KC, D])
        brt = sb("brt", [P, 1])
        bef = sb("bef", [P, P])
        ones = sb("ones", [P, P])
        iot = sb("iot", [P, CAP])
        wcol = sb("wcol", [P, B, NI])
        wts = sb("wts", [B * NI, P])
        wrow = sb("wrow", [B, S])
        wrest = sb("wrest", [B, 2, S])
        top = sb("top", [B, CAP // 8, 8])
        thr_r = sb("thr_r", [B, P])
        thr = sb("thr", [P, B])
        sel = sb("sel", [P, B, NI])
        fac = sb("fac", [P, B, NI])
        off = sb("off", [P, B, NI])
        pos = sb("pos", [P, B, NI])
        hot = sb("hot", [P, NI, B, CAP])
        hotw = sb("hotw", [P, NI, B, CAP])
        xg = sb("xg", [P, D])
        xgt = sb("xgt", [P, KC, P])
        hid = sb("hid", [P, DFF // P, P])
        blk = sb("blk", [P, D])
        spread = sb("spread", [P, NI, P])
        x1s = sb("x1s", [P, NT, D])
        hqk = sb("hqk", [P, 2, NI, 2, D1])
        res = sb("res", [P, 2, 2, NI, D1])
        nq = sb("nq", [P, 2, 2, NI, NST, D1], BF16)
        qt = sb("qt", [ST + 2, 4, S], BF16)
        kt = sb("kt", [ST + 2, 4, S], BF16)
        mxv = sb("mxv", [P, 2, 2, NI])
        mxm = sb("mxm", [P, NI])
        mhl = sb("mhl", [P, 2, NI], BF16)
        mrow = sb("mrow", [2 * NI, P], BF16)
        vb = sb("vb", [P, 4, NI, CGR])
        prob = sb("prob", [P, 4, S])
        acs = sb("acs", [P, S // 2])
        fol = sb("fol", [P, 2 * (D1 + 1)])
        rcs = sb("rcs", [P, 4, 2])
        ctt = sb("ctt", [P, 2, KC, P])
        ysb = sb("ysb", [P, 4, D])

        sc = ps("sc1", [P, 2, S])
        mx = [ps(f"mx{j}", [P, S // 2]) for j in range(2)]
        acc = ps("acc", [P, S // 2])
        misc = ps("misc", [P, S // 2])
        misc_b = misc[:, :].bitcast(BF16)

        ld_w, ld_x1, ld_br = sem("ld_w"), sem("ld_x1"), sem("ld_br")
        N_W = 8
        MOD = {n: k + 1 for order in ("wt thrt pos xg xgt hid spr blk", "xgs xgts hids sprs",
                                      "w wts thr thrs sel off idx hot hotw blks") for k, n in enumerate(order.split())}
        names = ("mod_pe mod_act mod_dve m_copy m_top m_fac set_dve1 set_pool1 "
                 "pool_g1 pool_g2 pool_g3 pool_g pe_tq pe_tk act_tq act_tk pe_m0 pe_m1 dve_m0 dve_m1 dve_mm dve_mh dve_ml "
                 "pe_c dve_c pe_x act_exp pe_pv act_acc pe_o dve_or dve_o "
                 "pe_ct act_ct pe_y dve_y dve_base").split()
        s_ = {n: sem(n) for n in names}
        row_st = sem("router_rows")
        hqk_ld = [sem(f"hqk_ld{j}") for j in range(2)]
        v_ld = [sem(f"vb_ld{j}") for j in range(4)]
        mr_st = [sem(f"max_placed{j}") for j in range(2)]
        y_st = [sem(f"y_stored{j}") for j in range(4)]

        block = ctx.enter_context(nc.Block())

        @block.sync
        def _(sp):
            sp.dma_start(brt[:, :], b_r.broadcast_to([P, 1])).then_inc(ld_br, 16)

            def mod(c, u):
                if (c, u) == (0, 2):
                    sp.wait_ge(s_["mod_dve"], MOD["wts"])
                    for b in range(B):
                        sp.dma_start(wrow[b:b + 1, :], wts[b * NI:(b + 1) * NI, :]).then_inc(row_st, 16)
                    sp.wait_ge(s_["set_pool1"], 1)
                if (c, u) == (1, 2):
                    sp.dma_start(bef[:, :], before).then_inc(ld_w, 16)
                    sp.dma_start(iot[:, :], slots.broadcast_to([P, CAP])).then_inc(ld_w, 16)
                    sp.dma_start(wt1[:, :, :], w1).then_inc(ld_w, 16)
                    sp.dma_start(bt1[:, :], b1).then_inc(ld_w, 16)
                    sp.dma_start(wt2[:, :, :], w2).then_inc(ld_w, 16)
                    sp.dma_start(bt2[:, :], b2.broadcast_to([P, D])).then_inc(ld_w, 16)
                    sp.dma_start(wou[:, :, :], w_out1).then_inc(ld_w, 16)
                    sp.dma_start(fol[:, :], fold).then_inc(ld_w, 16)
                    sp.dma_start(x1s[:, :, :], out.rearrange("(n p) d -> p n d", p=P)).then_inc(ld_x1, 16)

            def unit(T, u):
                if u == 0 and T.ok:
                    place, split = first(sp, T.n * (NI * 2 * D1)), T.n - 1
                    wait(sp, s_["pool_g"], split)
                    sp.dma_start(hqk[:, T.par, :, :, :].rearrange("p i j d -> p (i j d)"),
                                 qkv1_all[:, bass.ds(place, NI * 2 * D1)]).then_inc(hqk_ld[T.par], 16)
                t = T.back(3)
                if u == 1 and t.ok:
                    place, read = first(sp, t.n * (NI * D1) + n_qk), (t.n - 3) * 4
                    wait(sp, s_["pe_pv"], read)
                    sp.dma_start(vb[:, t.buf, :, 0:D1],
                                 qkv1_all[:, bass.ds(place, NI * D1)].rearrange("p (i d) -> p i d", i=NI)
                                 ).then_inc(v_ld[t.buf], 16)
                if u == 4 and t.ok:
                    wait(sp, s_["dve_c"], t.n + 1)
                    for r in range(2):
                        sp.dma_start(qt[ST + r:ST + r + 1, t.buf, :], mrow[r * NI:(r + 1) * NI, :]).then_inc(mr_st[r], 16)
                if T.m is None:
                    mod(T.c, u)

            items(sp, unit)
            for n in range(NT):
                sp.wait_ge(s_["dve_y"], n + 1)
                sp.dma_start(out[n * P:(n + 1) * P, :], ysb[:, n % 4, :]).then_inc(y_st[n % 4], 16)
            for j in range(4):
                sp.wait_ge(y_st[j], 16 * (NT // 4))

        @block.scalar
        def _(act):
            def ev(dst, src):
                return act.activation(dst, src, ACT.Copy)

            def mod(c, u):
                if (c, u) == (LAST, 1):
                    act.wait_ge(s_["mod_pe"], MOD["xg"])
                    ev(xg[:, :], mx[0][:, 0:D]).then_inc(s_["mod_act"], 1)
                if (c, u) == (LAST, 3):
                    act.wait_ge(s_["mod_pe"], MOD["xgt"])
                    ev(xgt[:, :, :], mx[1][:, 0:D].rearrange("p (k t) -> p k t", k=KC)).then_inc(s_["mod_act"], 1)
                if (c, u) == (LAST + 1, 0):
                    act.wait_ge(ld_w, 16 * N_W)
                    act.wait_ge(s_["mod_pe"], MOD["hid"])
                    for f in range(DFF // P):
                        ins = act.activation(hid[:, f, :], mx[f // 4][:, f % 4 * P:(f % 4 + 1) * P], ACT.Gelu_apprx_tanh,
                                             bias=bt1[:, f:f + 1])
                    ins.then_inc(s_["mod_act"], 1)
                if (c, u) == (LAST + 1, 2):
                    act.wait_ge(s_["mod_pe"], MOD["spr"])
                    for f in range(2):
                        ins = ev(spread[:, f * 4:f * 4 + 4, :], mx[f][:, :].rearrange("p (i t) -> p i t", i=4))
                    ins.then_inc(s_["mod_act"], 1)

            def unit(T, u):
                t = T.back(5)
                if u == 1 and t.ok:
                    act.wait_ge(s_["pe_pv"], t.n * 4 + 4)
                    wait(act, s_["pe_o"], t.n)
                    ev(acs[:, :], acc[:, :]).then_inc(s_["act_acc"], 1)
                t = T.back(4)
                if t.ok:
                    act.wait_ge(s_["pe_x"], t.n * NI + (u + 1))
                    wait(act, s_["pe_pv"], t.n * 4 + (u // 2 - 1))
                    act.activation(prob[:, u % 4, :], sc[:, u % 2, :], ACT.Exp,
                                   scale=D1 ** -0.5).then_inc(s_["act_exp"], 1)
                t = T.back(1)
                if u == 1 and t.ok:
                    act.wait_ge(s_["pe_tq"], t.n + 1)
                    wait(act, s_["pe_x"], (t.n - 3) * NI)
                    ev(qt[0:ST, t.buf, :], misc_b[0:ST, :]).then_inc(s_["act_tq"], 1)
                if u == 5 and t.ok:
                    act.wait_ge(s_["pe_tk"], t.n + 1)
                    wait(act, s_["pe_x"], (t.n - 3) * NI)
                    ev(kt[0:ST, t.buf, :], misc_b[0:ST, :]).then_inc(s_["act_tk"], 1)
                if T.m is None:
                    mod(T.c, u)

            items(act, unit)
            for n in range(NT):
                act.wait_ge(s_["pe_ct"], n + 1)
                wait(act, s_["pe_y"], n - 1)
                ev(ctt[:, n % 2, :, :], mx[n % 2][:, 0:D].rearrange("p (k t) -> p k t", k=KC)).then_inc(s_["act_ct"], 1)

        @block.vector
        def _(dve):
            dve.memset(ones[:, :], 1.0)
            dve.memset(kt[ST:ST + 2, :, :], 1.0)
            dve.tensor_copy(idb[:, :], idf[:, :]).then_inc(s_["set_dve1"], 1)
            dve.wait_ge(ld_br, 16)
            dve.tensor_tensor(wcol[:, :, :], xn2_all[:, :, D].rearrange("p (i b) -> p b i", b=B),
                              brt[:, :].unsqueeze(2).broadcast_to([P, B, NI]), ALU.add).then_inc(s_["mod_dve"], 1)
            dve.wait_ge(s_["mod_pe"], MOD["wt"])
            dve.tensor_copy(wts[:, :], mx[0][0:B * NI, 0:P]).then_inc(s_["mod_dve"], 1)

            def pick(k):
                rest = wrow if k == 0 else wrest[:, (k - 1) % 2, :]
                rest = rest[:, :] if k == 0 else rest
                if k == 0:
                    dve.wait_ge(row_st, 16 * B)
                else:
                    dve.wait_ge(s_["m_copy"], k)
                dve.max(top[:, k, :], rest).then_inc(s_["m_top"], 1)
                dve.wait_ge(s_["m_top"], k + 1)
                if k < CAP // 8 - 1:
                    dve.match_replace(wrest[:, k % 2, :], top[:, k, :], rest, NEVER).then_inc(s_["m_copy"], 1)
                else:
                    dve.tensor_copy(thr_r[:, :], top[:, k, 7:8].broadcast_to([B, P])).then_inc(s_["mod_dve"], 1)

            def mod(c, u):
                if c < NI and u == 7:
                    pick(c)
                if (c, u) == (LAST - 1, 1):
                    dve.wait_ge(ld_w, 16 * N_W)
                    dve.wait_ge(s_["mod_pe"], MOD["thrt"])
                    dve.tensor_copy(thr[:, :], mx[0][:, 0:B]).then_inc(s_["mod_dve"], 1)
                    dve.wait_ge(s_["mod_dve"], MOD["thrs"])
                    dve.tensor_tensor(sel[:, :, :], wcol[:, :, :], thr[:, :].unsqueeze(2).broadcast_to([P, B, NI]),
                                      ALU.is_gt).then_inc(s_["mod_dve"], 1)
                    dve.wait_ge(s_["mod_dve"], MOD["sel"])
                    dve.tensor_scalar(fac[:, :, :], sel[:, :, :], -1.0, 2.0, ALU.mult, ALU.add).then_inc(s_["m_fac"], 1)
                    dve.tensor_scalar(off[:, :, :], sel[:, :, :], -FAR, FAR, ALU.mult, ALU.add).then_inc(s_["mod_dve"], 1)
                if (c, u) == (LAST - 1, 3):
                    dve.wait_ge(s_["mod_dve"], MOD["off"])
                    dve.wait_ge(s_["mod_pe"], MOD["pos"])
                    dve.tensor_tensor(pos[:, :, :], mx[1][:, 0:B * NI].rearrange("p (b i) -> p b i", b=B), off[:, :, :],
                                      ALU.add).then_inc(s_["mod_dve"], 1)
                    dve.wait_ge(s_["mod_dve"], MOD["idx"])
                    hot_b = hot[:, :, :, :].rearrange("p i b c -> p b i c")
                    dve.tensor_tensor(hot_b, iot[:, :].unsqueeze(1).unsqueeze(1).broadcast_to([P, B, NI, CAP]),
                                      pos[:, :, :].unsqueeze(3).broadcast_to([P, B, NI, CAP]),
                                      ALU.is_equal).then_inc(s_["mod_dve"], 1)
                    dve.wait_ge(s_["mod_dve"], MOD["hot"])
                    dve.tensor_tensor(hotw[:, :, :, :].rearrange("p i b c -> p b i c"), hot_b,
                                      wcol[:, :, :].unsqueeze(3).broadcast_to([P, B, NI, CAP]),
                                      ALU.mult).then_inc(s_["mod_dve"], 1)
                if c == LAST and u < 4:
                    dve.wait_ge(s_["m_fac"], 1)
                    dve.wait_ge(ld_x1, 16)
                    for n in range(u * 4, u * 4 + 4):
                        dve.scalar_tensor_tensor(x1s[:, n, :], xn2_all[:, n, 0:D], fac[:, n % B, n // B:n // B + 1],
                                                 x1s[:, n, :], ALU.mult, ALU.add).then_inc(s_["dve_base"], 1)
                if (c, u) == (LAST + 1, 4):
                    dve.wait_ge(s_["mod_pe"], MOD["blk"])
                    dve.tensor_tensor(blk[:, :], mx[0][:, 0:D], bt2[:, :], ALU.add).then_inc(s_["mod_dve"], 1)

            def unit(T, u):
                t = T.back(2)
                if t.ok:
                    for h in range(2):
                        dve.wait_ge(s_[f"pe_m{h}"], t.n * NI + (u + 1))
                        if h == 0 and u == 0:
                            wait(dve, s_["dve_mm"], t.n - 1)
                        dve.tensor_reduce(mxv[:, t.par, h, u:u + 1], mx[h][:, :], AX.X, ALU.max
                                          ).then_inc(s_[f"dve_m{h}"], 1)
                t = T.back(3)
                if u == 0 and t.ok:
                    dve.wait_ge(s_["dve_m0"], t.n * NI + NI)
                    dve.wait_ge(s_["dve_m1"], t.n * NI + NI)
                    wait(dve, s_["dve_ml"], t.n)
                    dve.tensor_tensor(mxm[:, :], mxv[:, t.par, 0, :], mxv[:, t.par, 1, :], ALU.max).then_inc(s_["dve_mm"], 1)
                if u == 1 and t.ok:
                    dve.wait_ge(s_["dve_mm"], t.n + 1)
                    wait(dve, s_["pe_c"], t.n)
                    dve.tensor_scalar(mhl[:, 0, :], mxm[:, :], -1.0, None, ALU.mult).then_inc(s_["dve_mh"], 1)
                if u == 2 and t.ok:
                    dve.wait_ge(s_["dve_mh"], t.n + 1)
                    dve.scalar_tensor_tensor(mhl[:, 1, :], mxm[:, :], -1.0, mhl[:, 0, :], ALU.mult,
                                             ALU.subtract).then_inc(s_["dve_ml"], 1)
                if u == 3 and t.ok:
                    dve.wait_ge(s_["pe_c"], t.n + 1)
                    for r in range(2):
                        wait(dve, mr_st[r], t.n * 16)
                    dve.tensor_copy(mrow[:, :], misc_b[0:2 * NI, 0:P]).then_inc(s_["dve_c"], 1)
                t = T.back(5)
                if u == 7 and t.ok:
                    dve.wait_ge(s_["pe_o"], t.n + 1)
                    wait(dve, s_["dve_o"], t.n)
                    o = misc[:, 0:4 * 2 * (D1 + 1)].rearrange("p (t h e) -> p t h e", t=4, h=2)
                    dve.reciprocal(rcs[:, :, :], o[:, :, :, D1]).then_inc(s_["dve_or"], 1)
                    dve.wait_ge(s_["dve_or"], t.n + 1)
                    dve.tensor_tensor(ctxn[:, :, bass.ds(t.n * D1, D1)].rearrange("p (h t) e -> p t h e", h=2),
                                      o[:, :, :, 0:D1], rcs[:, :, :].unsqueeze(3).broadcast_to([P, 4, 2, D1]),
                                      ALU.mult).then_inc(s_["dve_o"], 1)
                if T.m is None:
                    mod(T.c, u)

            items(dve, unit)
            dve.wait_ge(s_["dve_base"], NT)
            for n in range(NT):
                dve.wait_ge(s_["pe_y"], n + 1)
                if n >= 4:
                    dve.wait_ge(y_st[n % 4], 16 * (n // 4))
                dve.tensor_tensor(ysb[:, n % 4, :], sc[:, n % 2, 0:D], x1s[:, n, :], ALU.add).then_inc(s_["dve_y"], 1)

        @block.gpsimd
        def _(pool):
            pool.memset(vb[:, :, :, D1 + 1:CGR], 0.0)
            pool.memset(vb[:, :, :, D1:D1 + 1], 1.0).then_inc(s_["set_pool1"], 1)

            pool.wait_ge(s_["set_dve1"], 1)
            one = ones[:, 0:NI * D1].rearrange("p (i d) -> p i d", i=NI)
            one2, one3 = (one.unsqueeze(2).broadcast_to([P, NI, k, D1]) for k in (2, 3))

            def unit(T, u):
                t = T
                if u != 0 or not t.ok:
                    return
                b = t.par
                both = hqk[:, b, :, :, :]
                hi = (nq[:, b, 0, :, 1:NST:2, :], nq[:, b, 1, :, 0:3, :])
                mid = (nq[:, b, 0, :, 2:NST:2, :], nq[:, b, 1, :, 3:5, :])
                low = (nq[:, b, 0, :, 0, :], nq[:, b, 1, :, 5, :])
                pool.wait_ge(hqk_ld[b], t.half * 16 + 16)
                wait(pool, s_["pe_tk"], t.n - 1)
                for j in range(2):
                    a = both[:, :, j, :].unsqueeze(2).broadcast_to([P, NI, 3, D1])
                    ins = pool.tensor_tensor(hi[j], a, one3, ALU.mult)
                ins.then_inc(s_["pool_g1"], 1)
                pool.wait_ge(s_["pool_g1"], t.n + 1)
                for j in range(2):
                    ins = pool.tensor_tensor(res[:, b, j, :, :], both[:, :, j, :], hi[j][:, :, 0, :], ALU.subtract)
                ins.then_inc(s_["pool_g2"], 1)
                pool.wait_ge(s_["pool_g2"], t.n + 1)
                for j in range(2):
                    a = res[:, b, j, :, :].unsqueeze(2).broadcast_to([P, NI, 2, D1])
                    ins = pool.tensor_tensor(mid[j], a, one2, ALU.mult)
                ins.then_inc(s_["pool_g3"], 1)
                pool.wait_ge(s_["pool_g3"], t.n + 1)
                for j in range(2):
                    ins = pool.tensor_tensor(low[j], res[:, b, j, :, :], mid[j][:, :, 0, :], ALU.subtract)
                ins.then_inc(s_["pool_g"], 1)

            items(pool, unit)

        @block.tensor
        def _(pe):
            pe.wait_ge(s_["set_dve1"], 1)
            pe.wait_ge(s_["mod_dve"], MOD["w"])
            pe.transpose(mx[0][0:B * NI, 0:P], wcol[:, :, :].rearrange("p b i -> p (b i)"), idf[:, :]
                         ).then_inc(s_["mod_pe"], 1)

            def mod(c, u):
                if (c, u) == (2, 0):
                    pe.wait_ge(s_["mod_dve"], MOD["wts"])
                if (c, u) == (4, 0):
                    pe.wait_ge(s_["set_pool1"], 1)
                    pe.wait_ge(ld_w, 16 * N_W)
                if (c, u) == (LAST - 1, 0):
                    pe.wait_ge(s_["mod_dve"], MOD["thr"])
                    for h in range(2):
                        pe.wait_ge(s_[f"dve_m{h}"], ITEMS * NI)
                    pe.transpose(mx[0][:, 0:B], thr_r[:, :], idf[0:B, 0:B]).then_inc(s_["mod_pe"], 1)
                if (c, u) == (LAST - 1, 2):
                    pe.wait_ge(s_["mod_dve"], MOD["sel"])
                    pe.matmul(mx[1][:, 0:B * NI], bef[:, :], sel[:, :, :].rearrange("p b i -> p (b i)"), start=True,
                              stop=False)
                    for b in range(B):
                        for i in range(NI - 1):
                            ins = pe.matmul(mx[1][:, b * NI + i + 1:(b + 1) * NI], ones[:, :],
                                            sel[:, b, i:i + 1].broadcast_to([P, NI - 1 - i]), start=False,
                                            stop=(b == B - 1 and i == NI - 2))
                    ins.then_inc(s_["mod_pe"], 1)
                if (c, u) == (LAST, 0):
                    pe.wait_ge(s_["mod_dve"], MOD["hot"])
                    for b in range(B):
                        for i in range(NI):
                            ins = pe.matmul(mx[0][b * CAP:(b + 1) * CAP, 0:D], hot[:, i, b, :], xn2_all[:, B * i + b, 0:D],
                                            start=(i == 0), stop=(i == NI - 1))
                    ins.then_inc(s_["mod_pe"], 1)
                if (c, u) == (LAST, 2):
                    pe.wait_ge(s_["mod_act"], MOD["xgs"])
                    for k in range(KC):
                        ins = pe.transpose(mx[1][:, k * P:(k + 1) * P], xg[:, k * P:(k + 1) * P], idf[:, :])
                    ins.then_inc(s_["mod_pe"], 1)
                if (c, u) == (LAST, 5):
                    pe.wait_ge(s_["mod_act"], MOD["xgts"])
                    for f in range(DFF // P):
                        for k in range(KC):
                            ins = pe.matmul(mx[f // 4][:, f % 4 * P:(f % 4 + 1) * P], wt1[:, k, f * P:(f + 1) * P],
                                            xgt[:, k, :], start=(k == 0), stop=(k == KC - 1))
                    ins.then_inc(s_["mod_pe"], 1)
                if (c, u) == (LAST + 1, 1):
                    pe.wait_ge(s_["mod_dve"], MOD["hotw"])
                    pe.wait_ge(s_["mod_act"], MOD["hids"])
                    for i in range(NI):
                        ins = pe.transpose(mx[i // 4][:, i % 4 * P:(i % 4 + 1) * P],
                                           hotw[:, i, :, :].rearrange("p b c -> p (b c)"), idf[:, :])
                    ins.then_inc(s_["mod_pe"], 1)
                if (c, u) == (LAST + 1, 3):
                    pe.wait_ge(s_["mod_act"], MOD["sprs"])
                    for f in range(DFF // P):
                        ins = pe.matmul(mx[0][:, 0:D], hid[:, f, :], wt2[:, f, :], start=(f == 0), stop=(f == DFF // P - 1))
                    ins.then_inc(s_["mod_pe"], 1)

            def unit(T, u):
                if T.m is None and T.c <= 4:
                    mod(T.c, u)
                x = T.back(4)
                if x.ok:
                    if u == 0:
                        for r in range(2):
                            pe.wait_ge(mr_st[r], x.n * 16 + 16)
                    wait(pe, s_["act_exp"], x.n * NI + (u - 1))
                    for h in range(2):
                        ins = pe.matmul(sc[:, u % 2, h * 512:(h + 1) * 512], kt[:, x.buf, u * P:(u + 1) * P],
                                        qt[:, x.buf, h * 512:(h + 1) * 512], start=True, stop=True)
                    ins.then_inc(s_["pe_x"], 1)
                t = T.back(2)
                if t.ok:
                    if u == 0:
                        pe.wait_ge(s_["act_tq"], t.n + 1)
                        pe.wait_ge(s_["act_tk"], t.n + 1)
                    for h in range(2):
                        wait(pe, s_[f"dve_m{h}"], t.n * NI + u)
                        pe.matmul(mx[h][:, :], qt[0:ST, t.buf, u * P:(u + 1) * P], kt[0:ST, t.buf, h * 512:(h + 1) * 512],
                                  start=True, stop=True).then_inc(s_[f"pe_m{h}"], 1)
                y = T.back(5) if u == 0 else x
                if u % 2 == 0 and y.ok:
                    p = u // 2 - 1 if u else 3
                    if p == 0:
                        pe.wait_ge(v_ld[y.buf], y.quarter * 16 + 16)
                        wait(pe, s_["act_acc"], y.n)
                    pe.wait_ge(s_["act_exp"], y.n * NI + (2 * p + 2))
                    for k in (2 * p, 2 * p + 1):
                        for h in range(2):
                            g = CGR * (2 * h + k % 2)
                            ins = pe.matmul(acc[g:g + CGR, :], vb[:, y.buf, k, :], prob[:, k % 4, h * 512:(h + 1) * 512],
                                            start=(p == 0), stop=(p == 3))
                    ins.then_inc(s_["pe_pv"], 1)
                t, c, o = T.back(1), T.back(3), T.back(5)
                if u == 1 and t.ok:
                    pe.wait_ge(s_["pool_g"], t.n + 1)
                    if t.back(4).ok:
                        wait(pe, s_["dve_o"], t.n - 4)
                    else:
                        wait(pe, s_["act_tk"], t.n)
                if u == 3 and c.ok:
                    pe.wait_ge(s_["dve_ml"], c.n + 1)
                    if t.ok:
                        pe.wait_ge(s_["act_tq"], t.n + 1)
                    else:
                        pe.wait_ge(s_["dve_o"], c.n - 2)
                    pe.transpose(misc_b[0:2 * NI, 0:P], mhl[:, :, :].rearrange("p r i -> p (r i)"),
                                 idb[:, :]).then_inc(s_["pe_c"], 1)
                if u == 5 and t.ok:
                    pe.wait_ge(s_["act_tq"], t.n + 1)
                    if c.ok:
                        pe.wait_ge(s_["dve_c"], c.n + 1)
                if u in (1, 5) and t.ok:
                    for i in range(NI):
                        ins = pe.transpose(misc_b[0:ST, i * P:(i + 1) * P],
                                           nq[:, t.par, u // 5, i, :, :].rearrange("p e d -> p (e d)"), idb[:, :])
                    ins.then_inc(s_["pe_tk" if u == 5 else "pe_tq"], 1)
                if u == 7 and o.ok:
                    pe.wait_ge(s_["act_acc"], o.n + 1)
                    if t.ok:
                        pe.wait_ge(s_["act_tk"], t.n + 1)
                    elif c.ok:
                        pe.wait_ge(s_["dve_c"], c.n + 1)
                    else:
                        pe.wait_ge(s_["dve_o"], o.n)
                    w = 2 * (D1 + 1)
                    for i in range(4):
                        ins = pe.matmul(misc[:, i * w:(i + 1) * w], acs[:, i * P:(i + 1) * P], fol[:, :],
                                        start=True, stop=True)
                    ins.then_inc(s_["pe_o"], 1)
                if T.m is None and T.c > 4:
                    mod(T.c, u)

            items(pe, unit)
            pe.wait_ge(s_["dve_o"], ITEMS)
            pe.wait_ge(s_["mod_dve"], MOD["blks"])
            for n in range(NT + 1):
                if n < NT:
                    i, b = n // B, n % B
                    wait(pe, s_["act_ct"], n - 1)
                    for c in range(KC):
                        ins = pe.transpose(mx[n % 2][:, c * P:(c + 1) * P],
                                           ctxn[:, i, b * D + c * P:b * D + (c + 1) * P], idf[:, :])
                    ins.then_inc(s_["pe_ct"], 1)
                if n > 0:
                    k = n - 1
                    i, b = k // B, k % B
                    pe.wait_ge(s_["act_ct"], k + 1)
                    wait(pe, s_["dve_y"], k - 1)
                    for c in range(KC):
                        pe.matmul(sc[:, k % 2, 0:D], ctt[:, k % 2, c, :], wou[:, c, :], start=(c == 0), stop=False)
                    pe.matmul(sc[:, k % 2, 0:D], spread[b * CAP:(b + 1) * CAP, i, :], blk[b * CAP:(b + 1) * CAP, :],
                              start=False, stop=True).then_inc(s_["pe_y"], 1)


def layouts(inputs):
    import numpy as np
    a = {k: np.asarray(v) for k, v in inputs.items()}
    c = np.ascontiguousarray
    x = a["L0_attn_x"].reshape(B, S // P, P, D).transpose(1, 0, 2, 3).reshape(B * S, D)
    w = a["L0_attn_w_qkv"]
    q, k, v = w[:HQ * HD].reshape(G, REP * HD, D), w[HQ * HD:(HQ + HKV) * HD].reshape(G, HD, D), \
        w[(HQ + HKV) * HD:].reshape(G, HD, D)
    w = np.concatenate([q, k, v], 1)
    w_qkv = w.transpose(2, 0, 1).reshape(KC, P, G, CW).transpose(1, 0, 2, 3)
    w_o = a["L0_attn_w_out"].T.reshape(G, 2, 2, HD, D).transpose(1, 3, 0, 2, 4).reshape(P, G, 2, D)
    w1 = a["L1_attn_W_in"].reshape(D, 3, H1, D1).transpose(0, 2, 1, 3)
    w1 = np.concatenate([w1[:, :, 0:2].reshape(D, 2 * D), w1[:, :, 2].reshape(D, D)], 1)
    up = lambda m: m.T.reshape(KC, P, G, HC).transpose(1, 0, 2, 3)
    return {
        "x": c(x), "w_qkv": c(w_qkv), "w_o": c(w_o),
        "q_w": c(a["L0_attn_q_norm_w"].reshape(1, HD)), "k_w": c(a["L0_attn_k_norm_w"].reshape(1, HD)),
        "w_gate": c(up(a["L0_ffn_wq_gate"])), "w_up": c(up(a["L0_ffn_wq_up"])),
        "s_gate": c(a["L0_ffn_s_gate"].reshape(G, HC).T), "s_up": c(a["L0_ffn_s_up"].reshape(G, HC).T),
        "w_down": c(a["L0_ffn_wq_down"].T.reshape(G, HC, D).transpose(1, 0, 2)),
        "s_down": c(a["L0_ffn_s_down"].reshape(1, D)),
        "ln_w": c(a["L1_attn_ln_w"].reshape(1, D)), "ln_b": c(a["L1_attn_ln_b"].reshape(1, D)),
        "w_in": c(w1.reshape(KC, P, 3 * D).transpose(1, 0, 2)),
        "w_r": c(a["L1_ffn_W_r"].reshape(1, D)),
        "w_out1": c(a["L1_attn_W_out"].reshape(KC, P, D).transpose(1, 0, 2)),
        "b_r": c(a["L1_ffn_b_r"].reshape(1, 1)),
        "w1": c(a["L1_ffn_W1"].reshape(KC, P, DFF).transpose(1, 0, 2)),
        "b1": c(a["L1_ffn_b1"].reshape(DFF // P, P).T),
        "w2": c(a["L1_ffn_W2"].reshape(DFF // P, P, D).transpose(1, 0, 2)),
        "b2": c(a["L1_ffn_b2"].reshape(1, D)),
    }


def constants():
    import numpy as np
    f = np.float32

    def angles(d, base=10000.0):
        inv = (f(1.0) / f(base) ** (np.arange(0, d, 2, dtype=f) / f(d))).astype(f)
        return np.arange(S, dtype=f)[:, None] * inv[None, :]

    e = angles(HD)
    cos, sin = np.cos(e), np.sin(e)
    r = np.repeat(angles(ROT1), 2, -1)
    sign = np.tile(np.array([-1, 1], f), ROT1 // 2)
    pos_table = np.concatenate([cos, cos, -sin, sin, np.cos(r), np.sin(r) * sign], -1).astype(f)
    key, query = np.arange(P)[:, None], np.arange(WIN)[None, :]
    outside = np.where((key > query) & (key <= query + WIN), 0, MASKED).astype(np.float16)
    masks = np.stack([np.stack([outside, outside], 1)] * 2)
    masks[0, 0:WIN, 0] = MASKED
    before = np.triu(np.ones((P, P), f), 1)
    fold = np.zeros((2, 2, CGR, 2, D1 + 1), f)
    for half in range(2):
        fold[half, :, 0:D1 + 1, half] = np.eye(D1 + 1, dtype=f)
    return {"pos_table": pos_table, "masks": masks, "eye": np.eye(P, dtype=f), "before": before,
            "fold": fold.reshape(P, 2 * (D1 + 1)), "slots": np.arange(CAP, dtype=f).reshape(1, CAP)}


INPUTS = ("x w_qkv w_o q_w k_w w_gate w_up s_gate s_up w_down s_down ln_w ln_b w_in w_r pos_table masks eye "
          "w_out1 b_r w1 b1 w2 b2 before fold slots").split()


def kernel(**inputs):
    import numpy as np
    import concourse.bacc as bacc
    from concourse.bass_utils import run_bass_kernel_spmd

    arrays = {**layouts(inputs), **constants()}
    nc = bacc.Bacc("TRN2", target_bir_lowering=False, num_devices=1)
    args = [nc.dram_tensor(n, arrays[n].shape, mybir.dt.from_np(arrays[n].dtype), kind="ExternalInput").ap()
            for n in INPUTS]
    out = nc.dram_tensor("out", (B * S, D), F32, kind="ExternalOutput").ap()
    build(nc, *args, out)
    r = run_bass_kernel_spmd(nc, [{n: arrays[n] for n in INPUTS}], core_ids=[0])
    tiles = r.results[0]["out"].reshape(NI, B, P, D)
    return np.ascontiguousarray(tiles.transpose(1, 0, 2, 3).reshape(B, S, D))
```
